# Optimizing a Trainium2 kernel written in Bass

```python
import numpy as np
import jax
import jax.numpy as jnp

def _softmax(x, axis=-1):
    return jax.nn.softmax(x, axis=axis)

def _gelu(x):
    return jax.nn.gelu(x, approximate=True)

def _silu(x):
    return jax.nn.silu(x)

def _sigmoid(x):
    return jax.nn.sigmoid(x)

def _layernorm(x, axis=-1, eps=1e-05):
    m = jnp.mean(x, axis=axis, keepdims=True)
    v = jnp.var(x, axis=axis, keepdims=True)
    return (x - m) / jnp.sqrt(v + eps)

def _scatter_add(tgt, idx, src, axis=0):
    return tgt.at[idx].add(src)

def _segment_sum(src, seg, n):
    return jax.ops.segment_sum(src, seg, n)
kernel_name = 'mk_vit_tower_d1_tok_img512_r4_0f24f9'

def setup_inputs(seed: int=0):
    np.random.seed(seed)
    _w = jnp.asarray

    def _rec_inputs():
        import jax
        import jax.numpy as jnp
        _rk = jax.random.key(seed)
        x = -0.000121822 + 0.999869 * jax.random.normal(jax.random.fold_in(_rk, 1), (64, 3, 196, 196), jnp.float32)
        return x
    x = _rec_inputs()

    def _L0_tok_setup():
        import jax, jax.numpy as jnp
        import numpy as np
        B, C, H, N_P, HID = (64, 3, 196, 14, 128)
        P = H // N_P
        IN_DIM = C * P * P
        SEQ = N_P * N_P + 1

        def sinusoidal_position(length, d):
            pos = jnp.arange(length, dtype=jnp.float32)[:, None]
            i = jnp.arange(d)[None, :]
            angle = pos / jnp.power(10000.0, (2 * (i // 2)).astype(jnp.float32) / d)
            return jnp.where(i % 2 == 0, jnp.sin(angle), jnp.cos(angle)).astype(jnp.float32)
        key = jax.random.key(seed)
        k_img, k_w, k_b, k_tok = jax.random.split(key, 4)
        img = jax.random.normal(k_img, (B, C, H, H), dtype=jnp.float32)
        W = jax.random.normal(k_w, (HID, IN_DIM), dtype=jnp.float32) / np.sqrt(IN_DIM)
        b = jax.random.normal(k_b, (HID,), dtype=jnp.float32) * 0.01
        token = jax.random.uniform(k_tok, (1, HID), dtype=jnp.float32)
        pos = sinusoidal_position(SEQ, HID)
        return {'img': img, 'W': W, 'b': b, 'token': token, 'pos': pos}
    _L0_tok_all = _L0_tok_setup()
    _L0_tok_in = {k: v for k, v in _L0_tok_all.items() if k in ('W', 'b', 'token', 'pos')}
    del _L0_tok_all

    def _L0_attn_setup():
        import jax, jax.numpy as jnp
        import numpy as np
        from jax import lax
        DIM = 128
        BATCH = 8
        SEQ = 512
        LR = 0.1
        DECAY = 0.9

        def _reference_tuple_inner(x, Wk, bk, Wv, bv, Wq, bq, Wo, bo):
            B, S, D = x.shape
            k = x @ Wk + bk
            v = x @ Wv + bv
            q = x @ Wq + bq
            state0 = jnp.zeros((B, D, D), dtype=x.dtype)

            def step(state, kvq):
                k_t, v_t, q_t = kvq
                mem = jnp.einsum('bd,bde->be', q_t, state)
                new_state = DECAY * state + LR * jnp.einsum('bd,be->bde', k_t, v_t)
                return (new_state, mem)
            kT = jnp.swapaxes(k, 0, 1)
            vT = jnp.swapaxes(v, 0, 1)
            qT = jnp.swapaxes(q, 0, 1)
            final_state, mems = lax.scan(step, state0, (kT, vT, qT))
            outputs = jnp.swapaxes(mems, 0, 1)
            out = outputs @ Wo + bo
            return (out, final_state)
        key = jax.random.key(seed)
        ks = jax.random.split(key, 5)
        scale = DIM ** (-0.5)
        return {'x': jax.random.normal(ks[0], (BATCH, SEQ, DIM), dtype=jnp.float32), 'Wk': jax.random.normal(ks[1], (DIM, DIM), dtype=jnp.float32) * scale, 'bk': jnp.zeros((DIM,), dtype=jnp.float32), 'Wv': jax.random.normal(ks[2], (DIM, DIM), dtype=jnp.float32) * scale, 'bv': jnp.zeros((DIM,), dtype=jnp.float32), 'Wq': jax.random.normal(ks[3], (DIM, DIM), dtype=jnp.float32) * scale, 'bq': jnp.zeros((DIM,), dtype=jnp.float32), 'Wo': jax.random.normal(ks[4], (DIM, DIM), dtype=jnp.float32) * scale, 'bo': jnp.zeros((DIM,), dtype=jnp.float32)}
    _L0_attn_all = _L0_attn_setup()
    _L0_attn_in = {k: v for k, v in _L0_attn_all.items() if k in ('Wk', 'bk', 'Wv', 'bv', 'Wq', 'bq', 'Wo', 'bo')}
    del _L0_attn_all

    def _L0_ffn_setup():
        import jax, jax.numpy as jnp
        import numpy as np
        D_MODEL = 128
        N_HEADS = 8
        KV_OPTS = (8, 4, 1)
        D_K = D_MODEL // N_HEADS

        def gqa(x, wq, wk, wv, wo, n_kv):
            B, S, _ = x.shape
            groups = N_HEADS // n_kv
            q = (x @ wq).reshape(B, S, N_HEADS, D_K).transpose(0, 2, 1, 3)
            k = (x @ wk).reshape(B, S, n_kv, D_K).transpose(0, 2, 1, 3)
            v = (x @ wv).reshape(B, S, n_kv, D_K).transpose(0, 2, 1, 3)
            k = jnp.repeat(k, groups, axis=1)
            v = jnp.repeat(v, groups, axis=1)
            scores = jnp.einsum('bhqd,bhkd->bhqk', q, k) / jnp.sqrt(jnp.float32(D_K))
            attn = jax.nn.softmax(scores, axis=-1)
            out = jnp.einsum('bhqk,bhkd->bhqd', attn, v)
            out = out.transpose(0, 2, 1, 3).reshape(B, S, D_MODEL)
            return out @ wo
        key = jax.random.key(seed)
        ks = jax.random.split(key, 32)
        it = iter(ks)
        s = 0.02
        inp = {'x': jax.random.normal(next(it), (64, 256, D_MODEL), dtype=jnp.float32)}
        inp['r_w1'] = jax.random.normal(next(it), (D_MODEL, D_MODEL // 4), jnp.float32) * s
        inp['r_b1'] = jnp.zeros((D_MODEL // 4,), jnp.float32)
        inp['r_w2'] = jax.random.normal(next(it), (D_MODEL // 4, len(KV_OPTS)), jnp.float32) * s
        inp['r_b2'] = jnp.zeros((len(KV_OPTS),), jnp.float32)
        for i, nkv in enumerate(KV_OPTS):
            inp[f'wq{i}'] = jax.random.normal(next(it), (D_MODEL, D_MODEL), jnp.float32) * s
            inp[f'wk{i}'] = jax.random.normal(next(it), (D_MODEL, nkv * D_K), jnp.float32) * s
            inp[f'wv{i}'] = jax.random.normal(next(it), (D_MODEL, nkv * D_K), jnp.float32) * s
            inp[f'wo{i}'] = jax.random.normal(next(it), (D_MODEL, D_MODEL), jnp.float32) * s
        return inp
    _L0_ffn_all = _L0_ffn_setup()
    _L0_ffn_in = {k: v for k, v in _L0_ffn_all.items() if k in ('r_w1', 'r_b1', 'r_w2', 'r_b2', 'wq0', 'wk0', 'wv0', 'wo0', 'wq1', 'wk1', 'wv1', 'wo1', 'wq2', 'wk2', 'wv2', 'wo2')}
    del _L0_ffn_all
    return {'x': x, 'L0_tok_W': _L0_tok_in['W'], 'L0_tok_b': _L0_tok_in['b'], 'L0_tok_token': _L0_tok_in['token'], 'L0_tok_pos': _L0_tok_in['pos'], 'L0_attn_Wk': _L0_attn_in['Wk'], 'L0_attn_bk': _L0_attn_in['bk'], 'L0_attn_Wv': _L0_attn_in['Wv'], 'L0_attn_bv': _L0_attn_in['bv'], 'L0_attn_Wq': _L0_attn_in['Wq'], 'L0_attn_bq': _L0_attn_in['bq'], 'L0_attn_Wo': _L0_attn_in['Wo'], 'L0_attn_bo': _L0_attn_in['bo'], 'L0_ffn_r_w1': _L0_ffn_in['r_w1'], 'L0_ffn_r_b1': _L0_ffn_in['r_b1'], 'L0_ffn_r_w2': _L0_ffn_in['r_w2'], 'L0_ffn_r_b2': _L0_ffn_in['r_b2'], 'L0_ffn_wq0': _L0_ffn_in['wq0'], 'L0_ffn_wk0': _L0_ffn_in['wk0'], 'L0_ffn_wv0': _L0_ffn_in['wv0'], 'L0_ffn_wo0': _L0_ffn_in['wo0'], 'L0_ffn_wq1': _L0_ffn_in['wq1'], 'L0_ffn_wk1': _L0_ffn_in['wk1'], 'L0_ffn_wv1': _L0_ffn_in['wv1'], 'L0_ffn_wo1': _L0_ffn_in['wo1'], 'L0_ffn_wq2': _L0_ffn_in['wq2'], 'L0_ffn_wk2': _L0_ffn_in['wk2'], 'L0_ffn_wv2': _L0_ffn_in['wv2'], 'L0_ffn_wo2': _L0_ffn_in['wo2']}

def reference(x, L0_tok_W, L0_tok_b, L0_tok_token, L0_tok_pos, L0_attn_Wk, L0_attn_bk, L0_attn_Wv, L0_attn_bv, L0_attn_Wq, L0_attn_bq, L0_attn_Wo, L0_attn_bo, L0_ffn_r_w1, L0_ffn_r_b1, L0_ffn_r_w2, L0_ffn_r_b2, L0_ffn_wq0, L0_ffn_wk0, L0_ffn_wv0, L0_ffn_wo0, L0_ffn_wq1, L0_ffn_wk1, L0_ffn_wv1, L0_ffn_wo1, L0_ffn_wq2, L0_ffn_wk2, L0_ffn_wv2, L0_ffn_wo2):
    import jax
    import jax.numpy as jnp

    def _L0_tok_ref(img, W, b, token, pos):
        import jax, jax.numpy as jnp
        import numpy as np
        B, C, H, N_P, HID = (64, 3, 196, 14, 128)
        P = H // N_P
        IN_DIM = C * P * P
        SEQ = N_P * N_P + 1

        def sinusoidal_position(length, d):
            pos = jnp.arange(length, dtype=jnp.float32)[:, None]
            i = jnp.arange(d)[None, :]
            angle = pos / jnp.power(10000.0, (2 * (i // 2)).astype(jnp.float32) / d)
            return jnp.where(i % 2 == 0, jnp.sin(angle), jnp.cos(angle)).astype(jnp.float32)
        Bn = img.shape[0]
        patches = img.reshape(Bn, C, N_P, P, N_P, P)
        patches = patches.transpose(0, 2, 4, 1, 3, 5).reshape(Bn, N_P * N_P, IN_DIM)
        tokens = jnp.einsum('bsd,hd->bsh', patches, W) + b
        cls = jnp.broadcast_to(token[None, :, :], (Bn, 1, HID))
        out = jnp.concatenate([cls, tokens], axis=1) + pos
        return out

    def _L0_attn_ref(x, Wk, bk, Wv, bv, Wq, bq, Wo, bo):
        import jax, jax.numpy as jnp
        import numpy as np
        from jax import lax
        DIM = 128
        BATCH = 8
        SEQ = 512
        LR = 0.1
        DECAY = 0.9

        def _reference_tuple_inner(x, Wk, bk, Wv, bv, Wq, bq, Wo, bo):
            B, S, D = x.shape
            k = x @ Wk + bk
            v = x @ Wv + bv
            q = x @ Wq + bq
            state0 = jnp.zeros((B, D, D), dtype=x.dtype)

            def step(state, kvq):
                k_t, v_t, q_t = kvq
                mem = jnp.einsum('bd,bde->be', q_t, state)
                new_state = DECAY * state + LR * jnp.einsum('bd,be->bde', k_t, v_t)
                return (new_state, mem)
            kT = jnp.swapaxes(k, 0, 1)
            vT = jnp.swapaxes(v, 0, 1)
            qT = jnp.swapaxes(q, 0, 1)
            final_state, mems = lax.scan(step, state0, (kT, vT, qT))
            outputs = jnp.swapaxes(mems, 0, 1)
            out = outputs @ Wo + bo
            return (out, final_state)
        return _reference_tuple_inner(x, Wk, bk, Wv, bv, Wq, bq, Wo, bo)[0]

    def _L0_ffn_ref(x, r_w1, r_b1, r_w2, r_b2, wq0, wk0, wv0, wo0, wq1, wk1, wv1, wo1, wq2, wk2, wv2, wo2):
        import jax, jax.numpy as jnp
        import numpy as np
        D_MODEL = 128
        N_HEADS = 8
        KV_OPTS = (8, 4, 1)
        D_K = D_MODEL // N_HEADS

        def gqa(x, wq, wk, wv, wo, n_kv):
            B, S, _ = x.shape
            groups = N_HEADS // n_kv
            q = (x @ wq).reshape(B, S, N_HEADS, D_K).transpose(0, 2, 1, 3)
            k = (x @ wk).reshape(B, S, n_kv, D_K).transpose(0, 2, 1, 3)
            v = (x @ wv).reshape(B, S, n_kv, D_K).transpose(0, 2, 1, 3)
            k = jnp.repeat(k, groups, axis=1)
            v = jnp.repeat(v, groups, axis=1)
            scores = jnp.einsum('bhqd,bhkd->bhqk', q, k) / jnp.sqrt(jnp.float32(D_K))
            attn = jax.nn.softmax(scores, axis=-1)
            out = jnp.einsum('bhqk,bhkd->bhqd', attn, v)
            out = out.transpose(0, 2, 1, 3).reshape(B, S, D_MODEL)
            return out @ wo
        routing_input = x.mean(axis=1)
        logits = jax.nn.relu(routing_input @ r_w1 + r_b1) @ r_w2 + r_b2
        sel = jnp.argmax(jax.nn.softmax(logits, axis=-1), axis=-1)
        params = [(wq0, wk0, wv0, wo0), (wq1, wk1, wv1, wo1), (wq2, wk2, wv2, wo2)]
        out = jnp.zeros_like(x)
        for i, nkv in enumerate(KV_OPTS):
            yi = gqa(x, *params[i], nkv)
            mask = (sel == i)[:, None, None]
            out = jnp.where(mask, yi, out)
        return out
    h = _L0_tok_ref(x, L0_tok_W, L0_tok_b, L0_tok_token, L0_tok_pos)
    h = h + _L0_attn_ref(_layernorm(h, axis=-1), L0_attn_Wk, L0_attn_bk, L0_attn_Wv, L0_attn_bv, L0_attn_Wq, L0_attn_bq, L0_attn_Wo, L0_attn_bo)
    h = h + _L0_ffn_ref(_layernorm(h, axis=-1), L0_ffn_r_w1, L0_ffn_r_b1, L0_ffn_r_w2, L0_ffn_r_b2, L0_ffn_wq0, L0_ffn_wk0, L0_ffn_wv0, L0_ffn_wo0, L0_ffn_wq1, L0_ffn_wk1, L0_ffn_wv1, L0_ffn_wo1, L0_ffn_wq2, L0_ffn_wk2, L0_ffn_wv2, L0_ffn_wo2)
    return h

_drawn_inputs = setup_inputs


def setup_inputs(seed=0):
    import zlib

    import numpy as np

    out = dict(_drawn_inputs(seed))
    spreads = {'L0_attn_bk': (0.0, 0.1),
     'L0_attn_bv': (0.0, 0.1),
     'L0_attn_bq': (0.0, 0.1),
     'L0_attn_bo': (0.0, 0.295),
     'L0_ffn_r_b1': (0.0, 0.8),
     'L0_ffn_r_b2': (0.0, 0.8)}
    factors = {'L0_ffn_wq2': 8.0, 'L0_ffn_wk2': 8.0, 'L0_ffn_wv2': 8.0, 'L0_ffn_wo2': 8.0}
    for name, (base, spread) in spreads.items():
        noise = np.random.default_rng([zlib.crc32(name.encode()), seed]).standard_normal(out[name].shape)
        drawn = base * np.exp(spread * noise) if base else spread * noise
        out[name] = jnp.asarray(drawn.astype(out[name].dtype))
    for name, factor in factors.items():
        out[name] = (out[name] * factor).astype(out[name].dtype)
    return out
```

```python
from contextlib import ExitStack

import concourse.bass as bass
from concourse import mybir

B, C, H, P, D = 64, 3, 196, 14, 128
N = H // P
S = N * N + 1
T = (S + 1) // 2
SP = 2 * T
IN = C * P * P
HEADS, DK = 8, 16
KV = (8, 4, 1)
ROWS = C * P
SHIFTS = 3
STEPS = (P + SHIFTS - 1) // SHIFTS
KROWS = SHIFTS * ROWS
WIDE = (N - 1) * P + STEPS
LR, DECAY, EPS = 0.1, 0.9, 1e-05
RING = 4
SPLIT = 4
BIAS_ROW = 96
CHUNK = 2 * SP

F32 = mybir.dt.float32
F32R = mybir.dt.float32r
I32 = mybir.dt.int32
ALU = mybir.AluOpType
ACT = mybir.ActivationFunctionType
AX = mybir.AxisListType


class Image:

    def __init__(self, round_, ring):
        self.round, self.ring = round_, ring

    @property
    def i(self):
        return self.round * RING + self.ring

    def back(self, lag):
        return Image(self.round + (self.ring - lag) // RING, (self.ring - lag) % RING)

    def exists(self):
        return not isinstance(self.round, int) or 0 <= self.i < B

    def has(self, earlier):
        return not isinstance(self.round, int) or self.i >= earlier


def run_slots(engine, slot, lag):
    for n in range(2 * RING):
        slot(Image(n // RING, n % RING))
    with engine.Fori(2, B // RING) as turn:
        for u in range(RING):
            slot(Image(turn, u))
    for n in range(B, B + lag):
        slot(Image(n // RING, n % RING))


def two(ap):
    return ap.rearrange("p (t e) -> p t e", t=2)


def prepare(nc, keep, ins):
    with ExitStack() as ctx:
        sb = lambda name, shape, dt=F32: ctx.enter_context(nc.sbuf_tensor(name, shape, dt))
        sem = lambda name: ctx.enter_context(nc.semaphore(name))
        w_rows = sb("w_rows", [128, IN])
        w_perm = sb("w_perm", [128, STEPS, 128])
        pos_rows = sb("pos_rows", [T, 2, D])
        token_col, b_col, bv_col = sb("token_col", [D, 1]), sb("b_col", [D, 1]), sb("bv_col", [D, 1])
        wv, wv_t, wo = sb("wv", [D, D]), sb("wv_t", [D, D]), sb("wo", [D, D])
        bv_wide = sb("bv_wide", [D, T])
        raw = [[sb(f"raw{i}{k}", [D, D if k in "qo" else n * DK]) for k in "qkvo"] for i, n in enumerate(KV)]
        steps_i, steps_f, base_t = sb("steps_i", [T, SP], I32), sb("steps_f", [T, SP]), sb("base_t", [T, SP])
        power = sb("power", [T, SP])
        ps = ctx.enter_context(nc.psum_tensor("prep_ps", [128, 8, 512], F32))
        loaded, pool_step, dve_step = sem("loaded"), sem("pool_step"), sem("dve_step")
        pe_step, act_step = sem("pe_step"), sem("act_step")
        loads = [
            (w_rows[:, :], ins["L0_tok_W"]),
            (b_col[:, :], ins["L0_tok_b"].rearrange("(d a) -> d a", a=1)),
            (token_col[:, :], ins["L0_tok_token"].rearrange("a d -> d a")),
            (pos_rows[:, 0, :], ins["L0_tok_pos"][0:T, :]),
            (pos_rows[0:S - T, 1, :], ins["L0_tok_pos"][T:S, :]),
            (keep["wq"][:, :], ins["L0_attn_Wq"]), (keep["wk"][:, :], ins["L0_attn_Wk"]),
            (wv[:, :], ins["L0_attn_Wv"]), (wo[:, :], ins["L0_attn_Wo"]),
            (keep["bq"][:, :], ins["L0_attn_bq"].rearrange("(d a) -> d a", a=1)),
            (keep["bk"][:, :], ins["L0_attn_bk"].rearrange("(d a) -> d a", a=1)),
            (bv_col[:, :], ins["L0_attn_bv"].rearrange("(d a) -> d a", a=1)),
            (keep["bo"][:, 0, :], ins["L0_attn_bo"].partition_broadcast(T)),
            (keep["bo"][:, 1, :], ins["L0_attn_bo"].partition_broadcast(T)),
            (keep["r_w1"][:, :], ins["L0_ffn_r_w1"]), (keep["r_w2"][:, :], ins["L0_ffn_r_w2"]),
            (keep["r_b1"][:, :], ins["L0_ffn_r_b1"].rearrange("(d a) -> d a", a=1)),
            (keep["r_b2"][:, :], ins["L0_ffn_r_b2"].partition_broadcast(B)),
        ]
        loads += [(raw[i][k][:, :], ins[f"L0_ffn_w{c}{i}"]) for i in range(len(KV)) for k, c in enumerate("qkvo")]
        block = ctx.enter_context(nc.Block())

        @block.sync
        def _(sp):
            for to, of in loads:
                sp.dma_start(to, of).then_inc(loaded, 16)
            sp.wait_ge(loaded, 16 * len(loads))

        @block.gpsimd
        def _(pool):
            ident = keep["ident"]
            nc.gpsimd.memset(ident[:, :], 0.0).then_inc(pool_step, 1)
            nc.gpsimd.iota(steps_i[:, :], pattern=[[1, SP]], base=-1, channel_multiplier=-1).then_inc(pool_step, 1)
            nc.gpsimd.memset(base_t[:, :], DECAY).then_inc(pool_step, 1)
            nc.gpsimd.memset(keep["half"][:, :], -0.5).then_inc(pool_step, 1)
            pool.wait_ge(pool_step, 4)
            nc.gpsimd.affine_select(out=ident[:, :], in_=ident[:, :], compare_op=ALU.not_equal, fill=1.0, base=0,
                                    pattern=[[-1, 128]], channel_multiplier=1).then_inc(pool_step, 1)
            nc.gpsimd.tensor_copy(steps_f[:, :], steps_i[:, :]).then_inc(pool_step, 1)
            pool.wait_ge(pool_step, 6)
            nc.gpsimd.tensor_tensor(power[:, :], base_t[:, :], steps_f[:, :], ALU.pow).then_inc(pool_step, 1)
            pool.wait_ge(pool_step, 7)
            nc.gpsimd.tensor_scalar(power[:, :], power[:, :], LR, None, ALU.mult).then_inc(pool_step, 1)
            pool.wait_ge(pool_step, 8)
            nc.gpsimd.affine_select(out=keep["mask"][:, 0:SP], in_=power[:, :], compare_op=ALU.is_ge, fill=0.0,
                                    base=-1, pattern=[[1, SP]], channel_multiplier=-1).then_inc(pool_step, 1)
            pool.wait_ge(pool_step, 9)
            nc.gpsimd.tensor_copy(keep["mask"][:, SP:SP + T], keep["mask"][:, 0:T]).then_inc(pool_step, 1)

        @block.vector
        def _(dve):
            nc.vector.memset(w_perm[:, :, :], 0.0).then_inc(dve_step, 1)
            dve.wait_ge(dve_step, 1)
            dve.wait_ge(loaded, 16 * len(loads))
            for g in range(SHIFTS):
                for s in range(STEPS):
                    if g * STEPS + s < P:
                        src = w_rows[:, :].rearrange("h (r j) -> h r j", j=P)[:, :, g * STEPS + s]
                        last = nc.vector.tensor_copy(w_perm[:, s, g * ROWS:(g + 1) * ROWS], src)
            last.then_inc(dve_step, 1)
            nc.vector.tensor_copy(bv_wide[:, :], bv_col[:, :].to_broadcast([D, T])).then_inc(dve_step, 1)
            for i, n in enumerate(KV):
                rep = HEADS // n
                sets = keep["sets"][:, i * 4 * D:(i + 1) * 4 * D].rearrange("p (w e) -> p w e", w=4)
                nc.vector.tensor_copy(sets[:, 0, :].rearrange("p (d h) -> p d h", d=DK),
                                      raw[i][0][:, :].rearrange("p (h d) -> p d h", d=DK))
                for g in range(rep):
                    nc.vector.tensor_copy(
                        sets[:, 1, :].rearrange("p (d r g) -> p d r g", d=DK, g=rep)[:, :, :, g],
                        raw[i][1][:, :].rearrange("p (r d) -> p d r", d=DK))
                    nc.vector.tensor_copy(
                        sets[:, 2, :].rearrange("p (r g d) -> p r g d", d=DK, g=rep)[:, :, g, :],
                        raw[i][2][:, :].rearrange("p (r d) -> p r d", d=DK))
                last = nc.vector.tensor_copy(sets[:, 3, :], raw[i][3][:, :])
            last.then_inc(dve_step, 1)
            dve.wait_ge(pe_step, 1)
            nc.vector.tensor_scalar(keep["add_t"][:, 1:S], ps[:, 6, 1:S], b_col[:, :], None, ALU.add)
            nc.vector.tensor_tensor(keep["add_t"][:, 0:1], ps[:, 6, 0:1], token_col[:, :], ALU.add).then_inc(dve_step, 1)

        @block.tensor
        def _(pe):
            pe.wait_ge(pool_step, 10)
            pe.wait_ge(dve_step, 3)
            pe.wait_ge(loaded, 16 * len(loads))
            ident = keep["ident"]
            nc.tensor.transpose(ps[:, 6, 0:T], pos_rows[:, 0, :], ident[0:T, 0:T])
            nc.tensor.transpose(ps[:, 6, T:S], pos_rows[0:S - T, 1, :], ident[0:S - T, 0:S - T]).then_inc(pe_step, 1)
            nc.tensor.transpose(ps[:, 5, 0:D], wv[:, :], ident[:, :]).then_inc(pe_step, 1)
            for s in range(STEPS):
                last = nc.tensor.transpose(ps[:, s, 0:D], w_perm[:, s, :], ident[:, :])
            last.then_inc(pe_step, 1)
            pe.wait_ge(act_step, 1)
            nc.tensor.matmul(ps[:, 7, 0:D], wv_t[:, :], wo[:, :], start=True, stop=True).then_inc(pe_step, 1)
            pe.wait_ge(act_step, 3)
            nc.tensor.matmul(ps[0:T, 7, 0:D], bv_wide[:, :], wo[:, :], start=True, stop=True).then_inc(pe_step, 1)

        @block.scalar
        def _(act):
            act.wait_ge(pe_step, 2)
            nc.scalar.activation(wv_t[:, :], ps[:, 5, 0:D], ACT.Copy).then_inc(act_step, 1)
            act.wait_ge(pe_step, 3)
            nc.scalar.activation(keep["w_tok"][:, :, :], ps[:, 0:STEPS, 0:D], ACT.Copy).then_inc(act_step, 1)
            act.wait_ge(pe_step, 4)
            nc.scalar.activation(keep["wvo"][:, :], ps[:, 7, 0:D], ACT.Copy).then_inc(act_step, 1)
            act.wait_ge(pe_step, 5)
            nc.scalar.activation(keep["bvo"][:, 0, :], ps[0:T, 7, 0:D], ACT.Copy)
            nc.scalar.activation(keep["bvo"][:, 1, :], ps[0:T, 7, 0:D], ACT.Copy).then_inc(act_step, 1)


def first(nc, keep, image):
    with ExitStack() as ctx:
        sb = lambda name, shape, dt=F32: ctx.enter_context(nc.sbuf_tensor(name, shape, dt))
        sem = lambda name: ctx.enter_context(nc.semaphore(name))
        ident, add_t, x2t, h1, sums = (keep[k] for k in ("ident", "add_t", "x2t", "h1", "sums"))
        img = [sb(f"img{j}", [KROWS, N, WIDE + STEPS]) for j in range(RING)]
        h0t = sb("h0t", [D, SP])
        xhat1, xhat2 = sb("xhat1", [T, 2, D]), sb("xhat2", [T, 2, D])
        x1t = sb("x1t", [D, SP])
        qkt = sb("qkt", [D, 2, SP])
        v1 = [sb(f"v1_{j}", [T, 2, D]) for j in range(2)]
        att = sb("att", [T, SP + T])
        stats1, stats2 = sb("stats1", [T, 2, 6]), sb("stats2", [T, 2, 6])
        mv1, mv2 = sb("mv1", [T, 2, 2]), sb("mv2", [T, 2, 2])
        var1, var2 = sb("var1", [T, 2]), sb("var2", [T, 2])
        rstd1, rstd2 = sb("rstd1", [T, 2]), sb("rstd2", [T, 2])
        ps = ctx.enter_context(nc.psum_tensor("ps", [128, 8, 512], F32))
        TOK, ROW, XT1, QK, VV, SC, OUT, XT2 = range(8)
        set_up = sem("set_up")
        img_in = [sem(f"img_in{j}") for j in range(RING)]
        patches_done, tokens_ready, tokens_rowed = sem("patches_done"), sem("tokens_ready"), sem("tokens_rowed")
        stats1_done, mv1_done, var1_done, rstd1_done = (sem(x) for x in ("stats1_done", "mv1_done", "var1_done", "rstd1_done"))
        kept, norm1_done, turned1, x1t_ready = (sem(x) for x in ("kept", "norm1_done", "turned1", "x1t_ready"))
        qk_done, v_done, qk_ready, v_ready = (sem(x) for x in ("qk_done", "v_done", "qk_ready", "v_ready"))
        scores_done, att_ready, out_done, h1_ready = (sem(x) for x in ("scores_done", "att_ready", "out_done", "h1_ready"))
        stats2_done, mv2_done, var2_done, rstd2_done = (sem(x) for x in ("stats2_done", "mv2_done", "var2_done", "rstd2_done"))
        norm2_done, turned2, x2t_ready = (sem(x) for x in ("norm2_done", "turned2", "x2t_ready"))
        IMG_DMAS = 16 * SHIFTS * C
        LAG = 6
        block = ctx.enter_context(nc.Block())

        def h1_of(b):
            return two(h1[:, bass.ds(b.i * 2 * D, 2 * D)])

        @block.sync
        def _(sp):
            sp.wait_ge(set_up, 1)

            def slot(b):
                if not b.exists():
                    return
                if b.has(RING):
                    sp.wait_ge(patches_done, b.i - RING + 1)
                for g in range(SHIFTS):
                    for c in range(C):
                        x0 = g * STEPS
                        cols = min(WIDE, H - x0)
                        src = image[bass.ds(b.i, 1), c, :, x0:x0 + cols].rearrange("a (i p) w -> (a p) i w", p=P)
                        r0 = g * ROWS + c * P
                        sp.dma_start(img[b.ring][r0:r0 + P, :, 0:cols], src).then_inc(img_in[b.ring], 16)
            run_slots(sp, slot, 0)

        @block.tensor
        def _(pe):
            pe.wait_ge(set_up, 1)

            def slot(n):
                b = n.back(6)
                if b.exists():
                    pe.wait_ge(norm2_done, b.i + 1)
                    if b.has(1):
                        pe.wait_ge(x2t_ready, b.i)
                    nc.tensor.transpose(ps[:, XT2, 0:T], xhat2[:, 0, :], ident[0:T, 0:T])
                    nc.tensor.transpose(ps[:, XT2, T:SP], xhat2[:, 1, :], ident[0:T, 0:T]).then_inc(turned2, 1)
                b = n.back(5)
                if b.exists():
                    pe.wait_ge(att_ready, b.i + 1)
                    pe.wait_ge(v_ready, b.i + 1)
                    if b.has(1):
                        pe.wait_ge(h1_ready, b.i)
                    v = v1[b.ring % 2]
                    nc.tensor.matmul(ps[0:T, OUT, 0:D], att[:, 0:T], v[:, 0, :], start=True, stop=True)
                    nc.tensor.matmul(ps[0:T, OUT, D:2 * D], att[:, T:SP], v[:, 0, :], start=True, stop=False)
                    nc.tensor.matmul(ps[0:T, OUT, D:2 * D], att[:, SP:SP + T], v[:, 1, :],
                                     start=False, stop=True).then_inc(out_done, 1)
                b = n.back(4)
                if b.exists():
                    pe.wait_ge(qk_ready, b.i + 1)
                    if b.has(1):
                        pe.wait_ge(att_ready, b.i)
                    nc.tensor.matmul(ps[0:T, SC, 0:SP], qkt[:, 1, 0:T], qkt[:, 0, :], start=True, stop=True)
                    nc.tensor.matmul(ps[0:T, SC, SP:SP + T], qkt[:, 1, T:SP], qkt[:, 0, T:SP],
                                     start=True, stop=True).then_inc(scores_done, 1)
                b = n.back(3)
                if b.exists():
                    pe.wait_ge(x1t_ready, b.i + 1)
                    if b.has(1):
                        pe.wait_ge(qk_ready, b.i)
                    nc.tensor.matmul(ps[:, QK, 0:SP], keep["wq"][:, :], x1t[:, :], start=True, stop=True)
                    nc.tensor.matmul(ps[:, QK, SP:2 * SP], keep["wk"][:, :], x1t[:, :],
                                     start=True, stop=True).then_inc(qk_done, 1)
                    if b.has(1):
                        pe.wait_ge(v_ready, b.i)
                    for t in range(2):
                        last = nc.tensor.matmul(ps[0:T, VV, t * D:(t + 1) * D], x1t[:, t * T:(t + 1) * T],
                                                keep["wvo"][:, :], start=True, stop=True)
                    last.then_inc(v_done, 1)
                b = n.back(2)
                if b.exists():
                    pe.wait_ge(norm1_done, b.i + 1)
                    if b.has(1):
                        pe.wait_ge(x1t_ready, b.i)
                    nc.tensor.transpose(ps[:, XT1, 0:T], xhat1[:, 0, :], ident[0:T, 0:T])
                    nc.tensor.transpose(ps[:, XT1, T:SP], xhat1[:, 1, :], ident[0:T, 0:T]).then_inc(turned1, 1)
                b = n.back(1)
                if b.exists():
                    pe.wait_ge(tokens_ready, b.i + 1)
                    if b.has(1):
                        pe.wait_ge(norm1_done, b.i)
                    nc.tensor.transpose(ps[0:T, ROW, 0:D], h0t[:, 0:T], ident[:, :])
                    nc.tensor.transpose(ps[0:T, ROW, D:2 * D], h0t[:, T:SP], ident[:, :]).then_inc(tokens_rowed, 1)
                b = n
                if b.exists():
                    pe.wait_ge(img_in[b.ring], IMG_DMAS * (b.round + 1))
                    if b.has(1):
                        pe.wait_ge(tokens_ready, b.i)
                    for s in range(STEPS):
                        cols = img[b.ring][:, :, s:s + (N - 1) * P + 1:P]
                        last = nc.tensor.matmul(ps[:, TOK, 0:S - 1].rearrange("p (i j) -> p i j", i=N),
                                                keep["w_tok"][0:KROWS, s, :], cols,
                                                start=(s == 0), stop=(s == STEPS - 1))
                    last.then_inc(patches_done, 1)
            run_slots(pe, slot, LAG)

        @block.vector
        def _(dve):
            nc.vector.tensor_copy(h0t[:, 0:1], add_t[:, 0:1])
            nc.vector.memset(h0t[:, S:SP], 0.0)
            nc.vector.memset(x1t[:, S:SP], 0.0)
            nc.vector.memset(x2t[:, :].rearrange("p (b s) -> p b s", b=B)[:, :, S:SP], 0.0)
            for j in range(RING):
                last = nc.vector.memset(img[j][:, :, H - (SHIFTS - 1) * STEPS:], 0.0)
            last.then_inc(set_up, 1)

            def slot(n):
                b = n.back(5)
                if b.exists():
                    dve.wait_ge(out_done, b.i + 1)
                    dve.wait_ge(kept, b.i + 1)
                    nc.vector.tensor_tensor(h1_of(b), two(ps[0:T, OUT, 0:2 * D]), h1_of(b), ALU.add).then_inc(h1_ready, 1)
                    dve.wait_ge(h1_ready, b.i + 1)
                b = n.back(4)
                if b.exists():
                    dve.wait_ge(scores_done, b.i + 1)
                    if b.has(1):
                        dve.wait_ge(out_done, b.i)
                    nc.vector.tensor_tensor(att[:, :], ps[0:T, SC, 0:SP + T], keep["mask"][:, :],
                                            ALU.mult).then_inc(att_ready, 1)
                b = n.back(5)
                if b.exists():
                    for t in range(2):
                        last = nc.vector.bn_stats(stats2[:, t, :], h1[:, bass.ds(b.i * 2 * D + t * D, D)])
                    last.then_inc(stats2_done, 1)
                    dve.wait_ge(stats2_done, b.i + 1)
                b = n.back(3)
                if b.exists():
                    dve.wait_ge(v_done, b.i + 1)
                    if b.has(2):
                        dve.wait_ge(out_done, b.i - 1)
                    nc.vector.tensor_tensor(v1[b.ring % 2][:, :, :], two(ps[0:T, VV, 0:2 * D]), keep["bvo"][:, :, :],
                                            ALU.add).then_inc(v_ready, 1)
                b = n.back(5)
                if b.exists():
                    for t in range(2):
                        last = nc.vector.bn_aggr(mv2[:, t, :], stats2[:, t, :])
                    last.then_inc(mv2_done, 1)
                    dve.wait_ge(mv2_done, b.i + 1)
                    nc.vector.tensor_scalar(var2[:, :], mv2[:, :, 1], EPS, None, ALU.add).then_inc(var2_done, 1)
                b = n.back(1)
                if b.exists():
                    dve.wait_ge(tokens_rowed, b.i + 1)
                    for t in range(2):
                        last = nc.vector.bn_stats(stats1[:, t, :], ps[0:T, ROW, t * D:(t + 1) * D])
                    last.then_inc(stats1_done, 1)
                    dve.wait_ge(stats1_done, b.i + 1)
                    nc.vector.tensor_tensor(h1_of(b), two(ps[0:T, ROW, 0:2 * D]), keep["bo"][:, :, :],
                                            ALU.add).then_inc(kept, 1)
                    for t in range(2):
                        last = nc.vector.bn_aggr(mv1[:, t, :], stats1[:, t, :])
                    last.then_inc(mv1_done, 1)
                    dve.wait_ge(mv1_done, b.i + 1)
                    nc.vector.tensor_scalar(var1[:, :], mv1[:, :, 1], EPS, None, ALU.add).then_inc(var1_done, 1)
                b = n.back(5)
                if b.exists():
                    dve.wait_ge(rstd2_done, b.i + 1)
                    if b.has(1):
                        dve.wait_ge(turned2, b.i)
                    for t in range(2):
                        last = nc.vector.tensor_scalar(xhat2[:, t, :], h1[:, bass.ds(b.i * 2 * D + t * D, D)],
                                                       mv2[:, t, 0:1], rstd2[:, t:t + 1], ALU.subtract, ALU.mult)
                    last.then_inc(norm2_done, 1)
                b = n.back(1)
                if b.exists():
                    dve.wait_ge(rstd1_done, b.i + 1)
                    if b.has(1):
                        dve.wait_ge(turned1, b.i)
                    for t in range(2):
                        last = nc.vector.tensor_scalar(xhat1[:, t, :], ps[0:T, ROW, t * D:(t + 1) * D],
                                                       mv1[:, t, 0:1], rstd1[:, t:t + 1], ALU.subtract, ALU.mult)
                    last.then_inc(norm1_done, 1)
                b = n
                if b.exists():
                    dve.wait_ge(patches_done, b.i + 1)
                    if b.has(1):
                        dve.wait_ge(tokens_rowed, b.i)
                    nc.vector.tensor_tensor(h0t[:, 1:S], ps[:, TOK, 0:S - 1], add_t[:, 1:S],
                                            ALU.add).then_inc(tokens_ready, 1)
            run_slots(dve, slot, LAG)

        @block.gpsimd
        def _(pool):
            def slot(n):
                b = n.back(5)
                if b.exists():
                    pool.wait_ge(var2_done, b.i + 1)
                    nc.gpsimd.tensor_tensor(rstd2[:, :], var2[:, :], keep["half"][:, :], ALU.pow).then_inc(rstd2_done, 1)
                b = n.back(1)
                if b.exists():
                    pool.wait_ge(var1_done, b.i + 1)
                    nc.gpsimd.tensor_tensor(rstd1[:, :], var1[:, :], keep["half"][:, :], ALU.pow).then_inc(rstd1_done, 1)
            run_slots(pool, slot, LAG)

        @block.scalar
        def _(act):
            act.wait_ge(set_up, 1)

            def slot(n):
                b = n.back(6)
                if b.exists():
                    act.wait_ge(turned2, b.i + 1)
                    nc.scalar.activation(x2t[:, bass.ds(b.i * SP, S)], ps[:, XT2, 0:S], ACT.Copy,
                                         accum_out=sums[:, bass.ds(b.i, 1)]).then_inc(x2t_ready, 1)
                b = n.back(3)
                if b.exists():
                    act.wait_ge(qk_done, b.i + 1)
                    if b.has(1):
                        act.wait_ge(scores_done, b.i)
                    nc.scalar.activation(qkt[:, 0, :], ps[:, QK, 0:SP], ACT.Identity, bias=keep["bq"][:, :])
                    nc.scalar.activation(qkt[:, 1, :], ps[:, QK, SP:2 * SP], ACT.Identity,
                                         bias=keep["bk"][:, :]).then_inc(qk_ready, 1)
                b = n.back(2)
                if b.exists():
                    act.wait_ge(turned1, b.i + 1)
                    if b.has(1):
                        act.wait_ge(v_done, b.i)
                    nc.scalar.activation(x1t[:, 0:S], ps[:, XT1, 0:S], ACT.Copy).then_inc(x1t_ready, 1)
            run_slots(act, slot, LAG)


def route(nc, keep):
    with ExitStack() as ctx:
        sb = lambda name, shape, dt=F32: ctx.enter_context(nc.sbuf_tensor(name, shape, dt))
        sem = lambda name: ctx.enter_context(nc.semaphore(name))
        HID, K = D // 4, len(KV)
        mean = sb("mean", [D, B])
        hidden = sb("hidden", [HID, B])
        logits, e, prob = sb("logits", [B, K]), sb("e", [B, K]), sb("prob_r", [B, K])
        nmax, total, rtotal = sb("nmax", [B, 1]), sb("total", [B, 1]), sb("rtotal", [B, 1])
        best12, not0, is2 = sb("best12", [B, 1]), sb("not0", [B, 1]), sb("is2", [B, 1])
        choice = sb("choice_col", [B, 128])
        ps = ctx.enter_context(nc.psum_tensor("route_ps", [128, 3, 512], F32))
        v, p, a = sem("route_v"), sem("route_p"), sem("route_a")
        block = ctx.enter_context(nc.Block())

        @block.vector
        def _(dve):
            nc.vector.memset(choice[:, :], 0.0)
            nc.vector.tensor_scalar(mean[:, :], keep["sums"][:, :], 1.0 / S, None, ALU.mult).then_inc(v, 1)
            dve.wait_ge(p, 1)
            nc.vector.tensor_scalar(hidden[:, :], ps[0:HID, 0, 0:B], keep["r_b1"][:, :], 0.0,
                                    ALU.add, ALU.max).then_inc(v, 1)
            dve.wait_ge(p, 2)
            nc.vector.tensor_tensor(logits[:, :], ps[0:B, 1, 0:K], keep["r_b2"][:, :], ALU.add).then_inc(v, 1)
            dve.wait_ge(v, 3)
            nc.vector.tensor_reduce(nmax[:, :], logits[:, :], AX.X, ALU.max, negate=True).then_inc(v, 1)
            dve.wait_ge(a, 1)
            nc.vector.reciprocal(rtotal[:, :], total[:, :]).then_inc(v, 1)
            dve.wait_ge(v, 5)
            nc.vector.tensor_scalar(prob[:, :], e[:, :], rtotal[:, :], None, ALU.mult).then_inc(v, 1)
            dve.wait_ge(v, 6)
            nc.vector.tensor_tensor(best12[:, :], prob[:, 1:2], prob[:, 2:3], ALU.max)
            nc.vector.tensor_tensor(is2[:, :], prob[:, 2:3], prob[:, 1:2], ALU.is_gt).then_inc(v, 1)
            dve.wait_ge(v, 7)
            nc.vector.tensor_tensor(not0[:, :], prob[:, 0:1], best12[:, :], ALU.is_lt).then_inc(v, 1)
            dve.wait_ge(v, 8)
            nc.vector.tensor_scalar(choice[:, 0:1], is2[:, :], 1.0, not0[:, :], ALU.add, ALU.mult).then_inc(v, 1)
            dve.wait_ge(p, 3)
            nc.vector.tensor_copy(keep["choice"][:, :], ps[0:1, 2, 0:B]).then_inc(v, 1)

        @block.scalar
        def _(act):
            act.wait_ge(v, 4)
            nc.scalar.activation(e[:, :], logits[:, :], ACT.Exp, bias=nmax[:, :], accum_out=total[:, :]).then_inc(a, 1)

        @block.tensor
        def _(pe):
            pe.wait_ge(v, 1)
            nc.tensor.matmul(ps[0:HID, 0, 0:B], keep["r_w1"][:, :], mean[:, :], start=True, stop=True).then_inc(p, 1)
            pe.wait_ge(v, 2)
            nc.tensor.matmul(ps[0:B, 1, 0:K], hidden[:, :], keep["r_w2"][:, :], start=True, stop=True).then_inc(p, 1)
            pe.wait_ge(v, 9)
            nc.tensor.transpose(ps[:, 2, 0:B], choice[:, :], keep["ident"][0:B, 0:B]).then_inc(p, 1)


def second(nc, keep, out):
    with ExitStack() as ctx:
        sb = lambda name, shape, dt=F32: ctx.enter_context(nc.sbuf_tensor(name, shape, dt))
        sem = lambda name: ctx.enter_context(nc.semaphore(name))
        ident, x2t, h1 = (keep[k] for k in ("ident", "x2t", "h1"))
        x_in = [sb(f"x_in{j}", [D, SP]) for j in range(RING)]
        w_in = [sb(f"w_in{j}", [D, 4, D]) for j in range(RING)]
        q_stack = [sb(f"q_stack{j}", [BIAS_ROW + 2, HEADS, SP], F32R) for j in range(RING)]
        k_stack = [sb(f"k_stack{j}", [BIAS_ROW + 2, HEADS, SP], F32R) for j in range(RING)]
        qk_hi = [sb(f"qk_hi{j}", [D, 2 * SP], F32R) for j in range(2)]
        qk_lo = [sb(f"qk_lo{j}", [D, 2 * SP], F32R) for j in range(2)]
        v_ones = [sb(f"v_ones{j}", [T, 2, HEADS, 2 * DK]) for j in range(2)]
        top = sb("top", [T, 2, HEADS])
        top_halves = sb("top_halves", [T, 2, 128])
        top_rows = [sb(f"top_rows{j}", [2 * HEADS, SP], F32R) for j in range(2)]
        prob = sb("prob", [T, 4, CHUNK])
        mix = sb("mix", [D, 2, SP])
        rsum = sb("rsum", [T, 4 * 4])
        mixed = sb("mixed", [T, 2, D])
        mixed_t = sb("mixed_t", [D, SP])
        h2 = [sb(f"h2_{j}", [T, 2, D]) for j in range(2)]
        ps = ctx.enter_context(nc.psum_tensor("ps2", [128, 8, 512], F32))
        QK, VT, M0, E0, MIX, FIN = 0, 1, 2, 4, 6, 7
        set_up = sem("set_up2")
        x_loaded = [sem(f"x_loaded{j}") for j in range(RING)]
        w_loaded = [sem(f"w_loaded{j}") for j in range(RING)]
        stacked = [sem(f"stacked{j}") for j in range(RING)]
        top_in = [sem(f"top_in{j}") for j in range(RING)]
        stored = [sem(f"stored{j}") for j in range(RING)]
        qk_done, hi_ready, lo_ready = sem("qk_done2"), sem("hi_ready"), sem("lo_ready")
        v_done, v_ready = sem("v_done2"), sem("v_ready2")
        m_done, m_read, top_done, split_hi, split_done = (sem(x) for x in ("m_done", "m_read", "top_done", "split_hi", "split_done"))
        top_turned, top_ready = sem("top_turned"), sem("top_ready")
        e_done, exp_done, pv_done = sem("e_done"), sem("exp_done"), sem("pv_done")
        mix_ready, mix_rowed, rsum_done, mixed_ready = (sem(x) for x in ("mix_ready", "mix_rowed", "rsum_done", "mixed_ready"))
        mixed_turned, mixed_t_ready, fin_done, h2_ready = (sem(x) for x in ("mixed_turned", "mixed_t_ready", "fin_done", "h2_ready"))
        STACK_DMAS = 16 * 2 * SPLIT
        LAG = 3
        block = ctx.enter_context(nc.Block())

        def keys(kt):
            return T if kt == 0 else S - T

        @block.sync
        def _(sp):
            sp.wait_ge(set_up, 1)

            def fetch(b):
                choice = sp.value_load(keep["choice"][0:1, bass.ds(b.i, 1)], min_val=0, max_val=len(KV) - 1)
                first_column = sp.snap(choice * 4 * D)
                if b.has(RING):
                    sp.wait_ge(v_done, b.i - RING + 1)
                sp.dma_start(x_in[b.ring][:, :], x2t[:, bass.ds(b.i * SP, SP)]).then_inc(x_loaded[b.ring], 16)
                if b.has(RING):
                    sp.wait_ge(fin_done, b.i - RING + 1)
                sp.dma_start(w_in[b.ring][:, :, :].rearrange("p w e -> p (w e)"),
                             keep["sets"][:, bass.ds(first_column, 4 * D)]).then_inc(w_loaded[b.ring], 16)

            def slot(n):
                b = n
                if b.exists():
                    fetch(b)
                    sp.wait_ge(hi_ready, b.i + 1)
                    hi, lo = qk_hi[b.ring % 2], qk_lo[b.ring % 2]
                    for half, qs, ks in ((hi, (0, 1), (0, 2)), (lo, (2, 3), (1, 3))):
                        if half is lo:
                            sp.wait_ge(lo_ready, b.i + 1)
                        for to, at, groups in ((q_stack, 0, qs), (k_stack, SP, ks)):
                            for s in groups:
                                sp.dma_start(to[b.ring][s * DK:(s + 1) * DK, :, :].bitcast(F32),
                                             half[:, at:at + SP].bitcast(F32)).then_inc(stacked[b.ring], 16)
                b = n.back(1)
                if b.exists():
                    sp.wait_ge(top_ready, b.i + 1)
                    sp.dma_start(q_stack[b.ring][BIAS_ROW:BIAS_ROW + 2, :, :].bitcast(F32),
                                 top_rows[b.ring % 2][:, :].bitcast(F32)).then_inc(top_in[b.ring], 16)
                b = n.back(3)
                if b.exists():
                    sp.wait_ge(h2_ready, b.i + 1)
                    for t in range(2):
                        sp.dma_start(out[bass.ds(b.i, 1), t * T:t * T + keys(t), :].rearrange("a s e -> (a s) e"),
                                     h2[b.ring % 2][0:keys(t), t, :]).then_inc(stored[b.ring], 16)
            run_slots(sp, slot, LAG)
            for j in range(RING):
                sp.wait_ge(stored[j], 32 * B // RING)

        @block.tensor
        def _(pe):
            pe.wait_ge(set_up, 1)

            def project_qk(b):
                pe.wait_ge(x_loaded[b.ring], 16 * (b.round + 1))
                pe.wait_ge(w_loaded[b.ring], 16 * (b.round + 1))
                if b.has(1):
                    pe.wait_ge(lo_ready, b.i)
                nc.tensor.matmul(ps[:, QK, 0:SP], w_in[b.ring][:, 0, :], x_in[b.ring][:, :], start=True, stop=True)
                nc.tensor.matmul(ps[:, QK, SP:2 * SP], w_in[b.ring][:, 1, :], x_in[b.ring][:, :],
                                 start=True, stop=True).then_inc(qk_done, 1)

            def project_v(b):
                if b.has(1):
                    pe.wait_ge(top_ready, b.i)
                for t in range(2):
                    last = nc.tensor.matmul(ps[0:T, VT, t * D:(t + 1) * D], x_in[b.ring][:, t * T:(t + 1) * T],
                                            w_in[b.ring][:, 2, :], start=True, stop=True)
                last.then_inc(v_done, 1)

            def max_scores(b, c):
                if c == 0:
                    pe.wait_ge(stacked[b.ring], STACK_DMAS * (b.round + 1))
                if b.has(1) or c >= 2:
                    pe.wait_ge(m_read, 8 * b.i + c - 1)
                qt = c // 4
                for j in range(2):
                    h = 2 * (c % 4) + j
                    last = nc.tensor.matmul(ps[0:T, M0 + c % 2, j * SP:(j + 1) * SP],
                                            q_stack[b.ring][0:BIAS_ROW, h, qt * T:(qt + 1) * T],
                                            k_stack[b.ring][0:BIAS_ROW, h, :], start=True, stop=True)
                last.then_inc(m_done, 1)

            def key_scores(b, c):
                if c == 0:
                    pe.wait_ge(top_in[b.ring], 16 * (b.round + 1))
                if b.has(1) or c >= 2:
                    pe.wait_ge(exp_done, 8 * b.i + c - 1)
                kt = (c // 2) % 2
                for j in range(2):
                    h = 4 * (c // 4) + 2 * (c % 2) + j
                    last = nc.tensor.matmul(ps[0:T, E0 + c % 2, j * SP:(j + 1) * SP],
                                            k_stack[b.ring][:, h, kt * T:(kt + 1) * T],
                                            q_stack[b.ring][:, h, :], start=True, stop=True)
                last.then_inc(e_done, 1)

            def mix_values(b, g, kt):
                if g == 0 and kt == 0:
                    pe.wait_ge(v_ready, b.i + 1)
                    if b.has(1):
                        pe.wait_ge(mix_ready, b.i)
                pe.wait_ge(exp_done, 8 * b.i + 4 * g + 2 * kt + 2)
                for j in range(4):
                    c = 4 * g + 2 * kt + j // 2
                    last = nc.tensor.matmul(ps[32 * j:32 * j + 32, MIX, g * SP:(g + 1) * SP],
                                            v_ones[b.ring % 2][0:keys(kt), kt, 4 * g + j, :],
                                            prob[0:keys(kt), c % 4, (j % 2) * SP:(j % 2 + 1) * SP],
                                            start=(kt == 0), stop=(kt == 1))
                last.then_inc(pv_done, 1)

            def turn_top(b):
                pe.wait_ge(split_done, b.i + 1)
                pe.wait_ge(v_ready, b.i + 1)
                for t in range(2):
                    last = nc.tensor.transpose(ps[:, VT, t * T:(t + 1) * T], top_halves[:, t, :], ident[0:T, 0:T])
                last.then_inc(top_turned, 1)

            def row_mix(b):
                pe.wait_ge(mix_ready, b.i + 1)
                if b.has(1):
                    pe.wait_ge(h2_ready, b.i)
                for t in range(2):
                    for g in range(2):
                        at = (2 * t + g) * D
                        last = nc.tensor.transpose(ps[0:T, FIN, at:at + D], mix[:, g, t * T:(t + 1) * T], ident[:, :])
                last.then_inc(mix_rowed, 1)

            def turn_mixed(b):
                pe.wait_ge(mixed_ready, b.i + 1)
                for t in range(2):
                    last = nc.tensor.transpose(ps[:, FIN, t * T:(t + 1) * T], mixed[:, t, :], ident[0:T, 0:T])
                last.then_inc(mixed_turned, 1)

            def project_out(b):
                pe.wait_ge(mixed_t_ready, b.i + 1)
                for t in range(2):
                    last = nc.tensor.matmul(ps[0:T, FIN, t * D:(t + 1) * D], mixed_t[:, t * T:(t + 1) * T],
                                            w_in[b.ring][:, 3, :], start=True, stop=True)
                last.then_inc(fin_done, 1)

            def slot(n):
                now, maxed, mixing, ending = n, n.back(1), n.back(2), n.back(3)
                plan = [
                    (project_qk, now), (max_scores, maxed, 0), (max_scores, maxed, 1),
                    (key_scores, mixing, 0), (key_scores, mixing, 1), (max_scores, maxed, 2),
                    (row_mix, ending), (max_scores, maxed, 3), (key_scores, mixing, 2), (key_scores, mixing, 3),
                    (max_scores, maxed, 4), (mix_values, mixing, 0, 0), (max_scores, maxed, 5),
                    (key_scores, mixing, 4), (key_scores, mixing, 5), (max_scores, maxed, 6),
                    (mix_values, mixing, 0, 1), (max_scores, maxed, 7), (turn_mixed, ending),
                    (key_scores, mixing, 6), (key_scores, mixing, 7), (turn_top, maxed),
                    (mix_values, mixing, 1, 0), (project_v, now), (project_out, ending), (mix_values, mixing, 1, 1),
                ]
                for step, b, *which in plan:
                    if b.exists():
                        step(b, *which)
            run_slots(pe, slot, LAG)

        @block.vector
        def _(dve):
            nc.vector.memset(top_halves[:, :, :], 0.0)
            for j in range(2):
                nc.vector.memset(v_ones[j][:, :, :, DK:], 1.0)
            for j in range(RING):
                nc.vector.memset(q_stack[j][SPLIT * DK:BIAS_ROW, :, :].bitcast(F32), 0.0)
                nc.vector.memset(k_stack[j][SPLIT * DK:BIAS_ROW, :, :].bitcast(F32), 0.0)
                last = nc.vector.memset(k_stack[j][BIAS_ROW:, :, :].bitcast(F32), 1.0)
            last.then_inc(set_up, 1)

            def low_halves(b):
                dve.wait_ge(hi_ready, b.i + 1)
                if b.has(2):
                    e = b.back(2)
                    dve.wait_ge(stacked[e.ring], STACK_DMAS * (e.round + 1))
                nc.vector.tensor_tensor(qk_lo[b.ring % 2][:, :], ps[:, QK, 0:2 * SP],
                                        qk_hi[b.ring % 2][:, :].bitcast(F32), ALU.subtract).then_inc(lo_ready, 1)

            def maximum(b, c):
                dve.wait_ge(m_done, 8 * b.i + c + 1)
                cols = ps[0:T, M0 + c % 2, 0:CHUNK].rearrange("p (h s) -> p h s", h=2)[:, :, 0:S]
                nc.vector.tensor_reduce(top[:, c // 4, 2 * (c % 4):2 * (c % 4) + 2], cols, AX.X, ALU.max,
                                        negate=True).then_inc(m_read, 1)

            def split_top(b):
                dve.wait_ge(m_read, 8 * b.i + 8)
                if b.has(1):
                    dve.wait_ge(top_turned, b.i)
                nc.vector.tensor_copy(top_halves[:, :, 0:HEADS].bitcast(F32R), top[:, :, :]).then_inc(split_hi, 1)
                dve.wait_ge(split_hi, b.i + 1)
                nc.vector.tensor_tensor(top_halves[:, :, HEADS:2 * HEADS], top[:, :, :], top_halves[:, :, 0:HEADS],
                                        ALU.subtract).then_inc(split_done, 1)

            def normalise(b):
                dve.wait_ge(mix_rowed, b.i + 1)
                view = ps[0:T, FIN, :].rearrange("p (x c) -> p x c", c=2 * DK)
                nc.vector.reciprocal(rsum[:, :], view[:, :, DK]).then_inc(rsum_done, 1)
                dve.wait_ge(rsum_done, b.i + 1)
                if b.has(1):
                    dve.wait_ge(mixed_turned, b.i)
                nc.vector.tensor_tensor(mixed[:, :, :].rearrange("p t (x c) -> p (t x) c", c=DK), view[:, :, 0:DK],
                                        rsum[:, :].unsqueeze(2).to_broadcast([T, 16, DK]),
                                        ALU.mult).then_inc(mixed_ready, 1)

            def finish(b):
                dve.wait_ge(fin_done, b.i + 1)
                if b.has(2):
                    e = b.back(2)
                    dve.wait_ge(stored[e.ring], 32 * (e.round + 1))
                nc.vector.tensor_tensor(h2[b.ring % 2][:, :, :], two(ps[0:T, FIN, 0:2 * D]),
                                        two(h1[:, bass.ds(b.i * 2 * D, 2 * D)]), ALU.add).then_inc(h2_ready, 1)

            def slot(n):
                now, maxed, ending = n, n.back(1), n.back(3)
                plan = [(maximum, maxed, 0), (low_halves, now), (maximum, maxed, 1), (maximum, maxed, 2),
                        (normalise, ending)]
                plan += [(maximum, maxed, c) for c in range(3, 8)]
                plan += [(split_top, maxed), (finish, ending)]
                for step, b, *which in plan:
                    if b.exists():
                        step(b, *which)
            run_slots(dve, slot, LAG)

        @block.scalar
        def _(act):
            act.wait_ge(set_up, 1)

            def high_halves(b):
                act.wait_ge(qk_done, b.i + 1)
                if b.has(2):
                    e = b.back(2)
                    act.wait_ge(stacked[e.ring], STACK_DMAS * (e.round + 1))
                nc.scalar.activation(qk_hi[b.ring % 2][:, :], ps[:, QK, 0:2 * SP], ACT.Copy).then_inc(hi_ready, 1)

            def exponent(b, c):
                act.wait_ge(e_done, 8 * b.i + c + 1)
                if b.has(1) or c >= 4:
                    act.wait_ge(pv_done, 4 * b.i + c // 2 - 1)
                nc.scalar.activation(prob[:, c % 4, :], ps[0:T, E0 + c % 2, 0:CHUNK], ACT.Exp,
                                     scale=DK ** -0.5).then_inc(exp_done, 1)

            def keep_mix(b):
                act.wait_ge(pv_done, 4 * (b.i + 1))
                if b.has(1):
                    act.wait_ge(mix_rowed, b.i)
                nc.scalar.activation(mix[:, :, :].rearrange("p g s -> p (g s)"), ps[:, MIX, 0:2 * SP],
                                     ACT.Copy).then_inc(mix_ready, 1)

            def keep_mixed_t(b):
                act.wait_ge(mixed_turned, b.i + 1)
                if b.has(1):
                    act.wait_ge(fin_done, b.i)
                nc.scalar.activation(mixed_t[:, :], ps[:, FIN, 0:SP], ACT.Copy).then_inc(mixed_t_ready, 1)

            def top_row(b):
                act.wait_ge(top_turned, b.i + 1)
                if b.has(2):
                    e = b.back(2)
                    act.wait_ge(top_in[e.ring], 16 * (e.round + 1))
                nc.scalar.activation(top_rows[b.ring % 2][:, :], ps[0:2 * HEADS, VT, 0:SP], ACT.Copy).then_inc(top_ready, 1)

            def keep_v(b):
                act.wait_ge(v_done, b.i + 1)
                if b.has(2):
                    act.wait_ge(pv_done, 4 * (b.i - 1))
                nc.scalar.activation(v_ones[b.ring % 2][:, :, :, 0:DK],
                                     ps[0:T, VT, 0:2 * D].rearrange("p (t h d) -> p t h d", t=2, d=DK),
                                     ACT.Copy).then_inc(v_ready, 1)

            def slot(n):
                now, maxed, mixing, ending = n, n.back(1), n.back(2), n.back(3)
                plan = [(keep_mix, ending), (high_halves, now)]
                plan += [(exponent, mixing, c) for c in range(6)]
                plan += [(keep_mixed_t, ending), (exponent, mixing, 6), (exponent, mixing, 7),
                         (top_row, maxed), (keep_v, now)]
                for step, b, *which in plan:
                    if b.exists():
                        step(b, *which)
            run_slots(act, slot, LAG)


def build(nc, ins, out):
    with ExitStack() as whole:
        sb = lambda name, shape, dt=F32: whole.enter_context(nc.sbuf_tensor(name, shape, dt))
        keep = {
            "ident": sb("ident", [128, 128]),
            "r_w1": sb("r_w1", [D, D // 4]), "r_b1": sb("r_b1", [D // 4, 1]),
            "r_w2": sb("r_w2", [D // 4, len(KV)]), "r_b2": sb("r_b2", [B, len(KV)]),
            "sets": sb("sets", [D, len(KV) * 4 * D]),
            "x2t": sb("x2t", [D, B * SP]), "h1": sb("h1", [T, B * 2 * D]),
            "sums": sb("sums", [D, B]), "choice": sb("choice", [1, B], I32),
        }
        with ExitStack() as part:
            sb = lambda name, shape: part.enter_context(nc.sbuf_tensor(name, shape, F32))
            keep |= {
                "mask": sb("mask", [T, SP + T]), "half": sb("half", [T, 2]),
                "w_tok": sb("w_tok", [128, STEPS, D]), "add_t": sb("add_t", [D, SP]),
                "wq": sb("wq", [D, D]), "wk": sb("wk", [D, D]), "wvo": sb("wvo", [D, D]),
                "bq": sb("bq", [D, 1]), "bk": sb("bk", [D, 1]),
                "bvo": sb("bvo", [T, 2, D]), "bo": sb("bo", [T, 2, D]),
            }
            prepare(nc, keep, ins)
            first(nc, keep, ins["x"])
        route(nc, keep)
        second(nc, keep, out)


INPUTS = ["x", "L0_tok_W", "L0_tok_b", "L0_tok_token", "L0_tok_pos",
          "L0_attn_Wk", "L0_attn_bk", "L0_attn_Wv", "L0_attn_bv", "L0_attn_Wq", "L0_attn_bq", "L0_attn_Wo", "L0_attn_bo",
          "L0_ffn_r_w1", "L0_ffn_r_b1", "L0_ffn_r_w2", "L0_ffn_r_b2",
          "L0_ffn_wq0", "L0_ffn_wk0", "L0_ffn_wv0", "L0_ffn_wo0",
          "L0_ffn_wq1", "L0_ffn_wk1", "L0_ffn_wv1", "L0_ffn_wo1",
          "L0_ffn_wq2", "L0_ffn_wk2", "L0_ffn_wv2", "L0_ffn_wo2"]


def kernel(**inputs):
    import numpy as np
    import concourse.bacc as bacc
    from concourse.bass_utils import run_bass_kernel_spmd

    nc = bacc.Bacc("TRN2", target_bir_lowering=False, num_devices=1)
    arrays, ins = {}, {}
    for name in INPUTS:
        a = np.ascontiguousarray(inputs[name])
        arrays[f"in_{name}"] = a
        ins[name] = nc.dram_tensor(f"in_{name}", a.shape, mybir.dt.from_np(a.dtype), kind="ExternalInput").ap()
    out = nc.dram_tensor("out", (B, S, D), F32, kind="ExternalOutput").ap()
    build(nc, ins, out)
    return run_bass_kernel_spmd(nc, [arrays], core_ids=[0]).results[0]["out"]
```
